# Optimizing a Trainium2 kernel written in Bass

```python
import numpy as np
import jax
import jax.numpy as jnp

def _softmax(x, axis=-1):
    return jax.nn.softmax(x, axis=axis)

def _gelu(x):
    return jax.nn.gelu(x, approximate=True)

def _silu(x):
    return jax.nn.silu(x)

def _sigmoid(x):
    return jax.nn.sigmoid(x)

def _layernorm(x, axis=-1, eps=1e-05):
    m = jnp.mean(x, axis=axis, keepdims=True)
    v = jnp.var(x, axis=axis, keepdims=True)
    return (x - m) / jnp.sqrt(v + eps)

def _scatter_add(tgt, idx, src, axis=0):
    return tgt.at[idx].add(src)

def _segment_sum(src, seg, n):
    return jax.ops.segment_sum(src, seg, n)
kernel_name = 'mk_cond_resid_d1_seqx_r2_c23976'

def setup_inputs(seed: int=0):
    np.random.seed(seed)
    _w = jnp.asarray

    def _rec_inputs():
        import jax
        import jax.numpy as jnp
        _rk = jax.random.key(seed)
        x = -0.0003929 + 0.9999 * jax.random.normal(jax.random.fold_in(_rk, 1), (8, 512, 512), jnp.float32)
        _lenS = 512 - jax.random.randint(jax.random.fold_in(_rk, 7), (8,), 0, max(1, 512 // 4) + 1, jnp.int32)
        _lenS2 = 512 - jax.random.randint(jax.random.fold_in(_rk, 8), (8,), 0, max(1, 512 // 4) + 1, jnp.int32)
        itok_B_0_2 = jax.random.randint(jax.random.fold_in(_rk, 11), (8,), 0, 3, jnp.int32)
        return (x, itok_B_0_2)
    x, itok_B_0_2 = _rec_inputs()

    def _L0_cond_setup():
        import jax, jax.numpy as jnp
        import numpy as np
        D_MODEL = 512
        D_FF = 2048
        N_EXPERTS = 5
        BATCH = 8
        SEQ = 1024

        def _gated_ffn(x, wi0, wi1, wo):
            g = jax.nn.gelu(x @ wi0, approximate=True)
            l = x @ wi1
            return g * l @ wo
        key = jax.random.key(seed)
        ks = jax.random.split(key, 12)
        s = 0.02
        inp = {'hidden_states': jax.random.normal(ks[0], (BATCH, SEQ, D_MODEL), jnp.float32), 'type_label': jax.random.randint(ks[1], (BATCH,), 0, N_EXPERTS, jnp.int32), 'Wi0': jax.random.normal(ks[2], (N_EXPERTS, D_MODEL, D_FF), jnp.float32) * s, 'Wi1': jax.random.normal(ks[3], (N_EXPERTS, D_MODEL, D_FF), jnp.float32) * s, 'Wo': jax.random.normal(ks[4], (N_EXPERTS, D_FF, D_MODEL), jnp.float32) * s, 'sWi0': jax.random.normal(ks[5], (D_MODEL, D_FF), jnp.float32) * s, 'sWi1': jax.random.normal(ks[6], (D_MODEL, D_FF), jnp.float32) * s, 'sWo': jax.random.normal(ks[7], (D_FF, D_MODEL), jnp.float32) * s, 'g0': jax.random.normal(ks[8], (2 * D_MODEL, D_MODEL), jnp.float32) * s, 'g1': jax.random.normal(ks[9], (D_MODEL, 2), jnp.float32) * s}
        return inp
    _L0_cond_all = _L0_cond_setup()
    _L0_cond_in = {k: v for k, v in _L0_cond_all.items() if k in ('Wi0', 'Wi1', 'Wo', 'sWi0', 'sWi1', 'sWo', 'g0', 'g1')}
    del _L0_cond_all
    return {'x': x, 'itok_B_0_2': itok_B_0_2, 'L0_cond_Wi0': _L0_cond_in['Wi0'], 'L0_cond_Wi1': _L0_cond_in['Wi1'], 'L0_cond_Wo': _L0_cond_in['Wo'], 'L0_cond_sWi0': _L0_cond_in['sWi0'], 'L0_cond_sWi1': _L0_cond_in['sWi1'], 'L0_cond_sWo': _L0_cond_in['sWo'], 'L0_cond_g0': _L0_cond_in['g0'], 'L0_cond_g1': _L0_cond_in['g1']}

def reference(x, itok_B_0_2, L0_cond_Wi0, L0_cond_Wi1, L0_cond_Wo, L0_cond_sWi0, L0_cond_sWi1, L0_cond_sWo, L0_cond_g0, L0_cond_g1):
    import jax
    import jax.numpy as jnp

    def _L0_cond_ref(hidden_states, type_label, Wi0, Wi1, Wo, sWi0, sWi1, sWo, g0, g1):
        import jax, jax.numpy as jnp
        import numpy as np
        D_MODEL = 512
        D_FF = 2048
        N_EXPERTS = 5
        BATCH = 8
        SEQ = 1024

        def _gated_ffn(x, wi0, wi1, wo):
            g = jax.nn.gelu(x @ wi0, approximate=True)
            l = x @ wi1
            return g * l @ wo
        share_out = _gated_ffn(hidden_states, sWi0, sWi1, sWo)
        wi0 = Wi0[type_label]
        wi1 = Wi1[type_label]
        wo = Wo[type_label]
        hg = jax.nn.gelu(jnp.einsum('bsd,bdf->bsf', hidden_states, wi0), approximate=True)
        hl = jnp.einsum('bsd,bdf->bsf', hidden_states, wi1)
        expert_out = jnp.einsum('bsf,bfd->bsd', hg * hl, wo)
        gate_in = jnp.concatenate([expert_out[:, 0], share_out[:, 0]], axis=-1)
        weights = jax.nn.softmax(jax.nn.relu(gate_in @ g0) @ g1, axis=-1)
        w0 = weights[:, 0][:, None, None]
        w1 = weights[:, 1][:, None, None]
        return expert_out * w0 + share_out * w1
    x = x + _L0_cond_ref(x, itok_B_0_2, L0_cond_Wi0, L0_cond_Wi1, L0_cond_Wo, L0_cond_sWi0, L0_cond_sWi1, L0_cond_sWo, L0_cond_g0, L0_cond_g1)
    return x

_drawn_inputs = setup_inputs


def setup_inputs(seed=0):
    import zlib

    import numpy as np

    out = dict(_drawn_inputs(seed))
    spreads = {}
    factors = {'L0_cond_g0': 8.0, 'L0_cond_g1': 8.0}
    for name, (base, spread) in spreads.items():
        noise = np.random.default_rng([zlib.crc32(name.encode()), seed]).standard_normal(out[name].shape)
        drawn = base * np.exp(spread * noise) if base else spread * noise
        out[name] = jnp.asarray(drawn.astype(out[name].dtype))
    for name, factor in factors.items():
        out[name] = (out[name] * factor).astype(out[name].dtype)
    return out
```

```python
from contextlib import ExitStack

import concourse.bass as bass
from concourse import mybir

F32 = mybir.dt.float32
F32R = mybir.dt.float32r
I32 = mybir.dt.int32
ALU = mybir.AluOpType
ACT = mybir.ActivationFunctionType
AX = mybir.AxisListType
RADD = bass.bass_isa.ReduceOp.add

P = 128
RAW_SLOTS = 4
HI, LO = 0, 1
PASSES = [(LO, HI), (HI, LO), (HI, HI)]


def build(nc, x_cols, x_rows, labels, experts, shared, g0_rows, g1_rows, out):
    BATCH, _, KC, TOK = x_cols.shape
    N_EXPERTS, CHUNKS, _, CHUNK_W = experts.shape
    D = KC * P
    MC = TOK // P
    WI = 2 * D
    WO = D
    NC = g0_rows.shape[1]
    assert CHUNK_W == WI + WO and CHUNKS % RAW_SLOTS == 0 and BATCH % 2 == 0
    GROUPS = CHUNKS // RAW_SLOTS
    PAIRS = BATCH // 2

    with ExitStack() as ctx:
        def sb(name, shape, dt=F32):
            return ctx.enter_context(nc.sbuf_tensor(name, shape, dt))

        def sem(name):
            return ctx.enter_context(nc.semaphore(name))

        raw = [sb(f"raw{r}", [P, CHUNK_W]) for r in range(RAW_SLOTS)]
        wi = [[sb(f"wi{s}{p}", [P, 2, KC, P], F32R) for p in "hl"] for s in range(2)]
        wo = [[sb(f"wo{s}{p}", [P, D], F32R) for p in "hl"] for s in range(2)]
        x_raw = sb("x_raw", [P, KC, TOK])
        xs = [[sb(f"x{s}{p}", [P, KC, TOK], F32R) for p in "hl"] for s in range(2)]
        act = [sb(f"act{s}", [P, TOK]) for s in range(2)]
        hid = [sb(f"hid{s}", [P, TOK]) for s in range(2)]
        hs = [[sb(f"hid{s}{p}", [P, TOK], F32R) for p in "hl"] for s in range(2)]
        e_out = sb("e_out", [P, MC, D])
        s_out = sb("s_out", [P, MC, D])
        x_res = sb("x_res", [P, MC, D])
        mix = sb("mix", [P, MC, D])
        g0_sb = sb("g0_sb", [P, NC, 2, D])
        g1_sb = sb("g1_sb", [P, 2, NC])
        gate_row = sb("gate_row", [P, 2, D])
        gate_prod = sb("gate_prod", [P, NC, D])
        gate_sum = sb("gate_sum", [P, 2, NC])
        gate_act = sb("gate_act", [P, NC])
        logit_prod = sb("logit_prod", [P, 2, NC])
        logit_part = sb("logit_part", [P, 2])
        logits = sb("logits", [P, 2])
        logit_max = sb("logit_max", [P, 1])
        logit_diff = sb("logit_diff", [P, 2])
        gate_exp = sb("gate_exp", [P, 2])
        gate_den = sb("gate_den", [P, 1])
        gate_inv = sb("gate_inv", [P, 1])
        gate_w = sb("gate_w", [P, 2])
        labels_sb = sb("labels_sb", [1, BATCH], I32)

        def bank(name):
            return ctx.enter_context(nc.psum_tensor(name, [P, 512], F32))

        ps_gate = [bank(f"ps_gate{s}") for s in range(2)]
        ps_lin = [bank(f"ps_lin{s}") for s in range(2)]
        ps_out = [bank(f"ps_out{m}") for m in range(MC)]

        raw_loaded = [sem(f"raw_loaded{r}") for r in range(RAW_SLOTS)]
        labels_loaded = sem("labels_loaded")
        gate_weights_loaded = sem("gate_weights_loaded")
        x_raw_loaded = sem("x_raw_loaded")
        x_res_loaded = sem("x_res_loaded")
        out_stored = sem("out_stored")
        x_hi_done = sem("x_hi_done")
        x_ready = sem("x_ready")
        wi_hi_done = sem("wi_hi_done")
        wi_ready = sem("wi_ready")
        wo_hi_done = sem("wo_hi_done")
        wo_ready = sem("wo_ready")
        gate_projected = sem("gate_projected")
        lin_projected = sem("lin_projected")
        gelu_done = sem("gelu_done")
        product_done = sem("product_done")
        hid_hi_done = sem("hid_hi_done")
        hid_ready = sem("hid_ready")
        down_done = sem("down_done")
        out_copied_act = sem("out_copied_act")
        out_copied_dve = sem("out_copied_dve")
        row_spread = sem("row_spread")
        gate_step = sem("gate_step")
        logits_part_done = sem("logits_part_done")
        logits_done = sem("logits_done")
        logits_shifted = sem("logits_shifted")
        max_done = sem("max_done")
        exp_done = sem("exp_done")
        weight_step = sem("weight_step")
        mixed = sem("mixed")

        block = ctx.enter_context(nc.Block())

        def schedule(eng, expert, shared_):
            expert(0, 0, first=True)
            with eng.Fori(0, PAIRS - 1) as i:
                shared_(i * 2, 0)
                expert(i * 2 + 1, 1)
                shared_(i * 2 + 1, 1)
                expert(i * 2 + 2, 0)
            shared_(BATCH - 2, 0)
            expert(BATCH - 1, 1, last=True)
            shared_(BATCH - 1, 1, last=True)

        @block.sync
        def _(sp):
            def load_pass(weights, t0, first, between):
                def group(g, wait):
                    for r in range(RAW_SLOTS):
                        if wait:
                            sp.wait_ge(wo_ready, t0 + g * RAW_SLOTS + (r + 1 - RAW_SLOTS))
                        sp.dma_start(raw[r][:, :], weights(g * RAW_SLOTS + r)).then_inc(raw_loaded[r], 16)

                group(0, not first)
                between()
                with sp.Fori(1, GROUPS) as g:
                    group(g, True)

            def expert(b, slot, first=False, last=False):
                label = sp.value_load(labels_sb[0:1, bass.ds(b, 1)], min_val=0, max_val=N_EXPERTS - 1)

                def next_x():
                    sp.wait_ge(x_ready, b + 1)
                    sp.dma_start(x_raw[:, :, :], x_cols[bass.ds(b + 1, 1)].rearrange("b p k s -> (b p) k s")
                                 ).then_inc(x_raw_loaded, 16)

                load_pass(lambda c: experts[bass.ds(label, 1), bass.ds(c, 1)].rearrange("e c p w -> (e c p) w"),
                          b * (2 * CHUNKS), first, (lambda: None) if last else next_x)
                if not first:
                    store(b - 1)
                    sp.wait_ge(out_stored, b * 16)
                sp.dma_start(x_res[:, :, :], x_rows[bass.ds(b, 1)].rearrange("b p m d -> (b p) m d")
                             ).then_inc(x_res_loaded, 16)

            def shared_(b, slot, last=False):
                load_pass(lambda c: shared[bass.ds(c, 1)].rearrange("c p w -> (c p) w"),
                          b * (2 * CHUNKS) + CHUNKS, False, lambda: None)

            def store(b):
                sp.wait_ge(mixed, b * 2 + 2)
                sp.dma_start(out[bass.ds(b, 1)].rearrange("b p m d -> (b p) m d"), mix[:, :, :]
                             ).then_inc(out_stored, 16)

            sp.dma_start(labels_sb[:, :], labels).then_inc(labels_loaded, 16)
            sp.dma_start(x_raw[:, :, :], x_cols[0]).then_inc(x_raw_loaded, 16)
            sp.dma_start(g0_sb[:, :, :, :], g0_rows).then_inc(gate_weights_loaded, 16)
            sp.dma_start(g1_sb[:, :, :], g1_rows).then_inc(gate_weights_loaded, 16)
            sp.wait_ge(labels_loaded, 16)
            schedule(sp, expert, shared_)
            store(BATCH - 1)
            sp.wait_ge(out_stored, 16 * BATCH)

        @block.tensor
        def _(pe):
            def project(t, s, xslot, first=False):
                pe.wait_ge(wi_ready, t + 1)
                for which, bank_, free, done in ((0, ps_gate[s], gelu_done, gate_projected),
                                                 (1, ps_lin[s], product_done, lin_projected)):
                    if not first:
                        pe.wait_ge(free, t - 1)
                    for n, (wp, xp) in enumerate(PASSES):
                        for k in range(KC):
                            mm = nc.tensor.matmul(bank_[:, :], wi[s][wp][:, which, k, :], xs[xslot][xp][:, k, :],
                                                  start=(n == 0 and k == 0), stop=(n == 2 and k == KC - 1))
                    mm.then_inc(done, 1)

            def back(t, s, start=False, stop=False):
                pe.wait_ge(hid_ready, t + 1)
                pe.wait_ge(wo_ready, t + 1)
                for m in range(MC):
                    for n, (hp, wp) in enumerate(PASSES):
                        mm = nc.tensor.matmul(ps_out[m][:, :], hs[s][hp][:, m * P:(m + 1) * P], wo[s][wp][:, :],
                                              start=(start and n == 0), stop=(stop and n == 2),
                                              skip_group_check=True)
                mm.then_inc(down_done, 1)

            def run_pass(number, xslot, next_xslot, next_batch, first=False, last=False):
                t0 = number * CHUNKS
                project(t0 + 1, 1, xslot, first)
                if not first:
                    pe.wait_ge(out_copied_act, number)
                    pe.wait_ge(out_copied_dve, number)
                back(t0, 0, start=True)
                with pe.Fori(1, CHUNKS // 2) as j:
                    project(t0 + j * 2, 0, xslot)
                    back(t0 + j * 2 - 1, 1)
                    project(t0 + j * 2 + 1, 1, xslot)
                    back(t0 + j * 2, 0)
                if not last:
                    if next_batch is not None:
                        pe.wait_ge(x_ready, next_batch + 1)
                    project(t0 + CHUNKS, 0, next_xslot)
                back(t0 + CHUNKS - 1, 1, stop=True)

            def expert(b, slot, first=False, last=False):
                run_pass(b * 2, slot, slot, None, first)

            def shared_(b, slot, last=False):
                run_pass(b * 2 + 1, slot, 1 - slot, b + 1, last=last)

            pe.wait_ge(x_ready, 1)
            project(0, 0, 0, first=True)
            schedule(pe, expert, shared_)

        @block.scalar
        def _(sc):
            def split_x(b, slot):
                sc.wait_ge(x_raw_loaded, b * 16 + 16)
                nc.scalar.copy(xs[slot][HI][:, :, :], x_raw[:, :, :]).then_inc(x_hi_done, 1)

            def split_wi(t, lap, r, free):
                sc.wait_ge(raw_loaded[r], lap * 16 + 16)
                if free:
                    sc.wait_ge(lin_projected, t - 1)
                nc.scalar.copy(wi[r % 2][HI][:, :, :, :].rearrange("p a k f -> p (a k f)"), raw[r][:, 0:WI]
                               ).then_inc(wi_hi_done, 1)

            def split_wo(t, r, free):
                if free:
                    sc.wait_ge(down_done, t - 1)
                nc.scalar.copy(wo[r % 2][HI][:, :], raw[r][:, WI:CHUNK_W]).then_inc(wo_hi_done, 1)

            def chunk(t, lap, r, start=False, more=2):
                s = r % 2
                sc.wait_ge(gate_projected, t + 1)
                if not start:
                    sc.wait_ge(product_done, t - 1)
                nc.scalar.activation(act[s][:, :], ps_gate[s][:, :], ACT.Gelu_apprx_tanh).then_inc(gelu_done, 1)
                sc.wait_ge(product_done, t + 1)
                if not start:
                    sc.wait_ge(down_done, t - 1)
                nc.scalar.copy(hs[s][HI][:, :], hid[s][:, :]).then_inc(hid_hi_done, 1)
                if more >= 2:
                    split_wi(t + 2, lap + (r + 2) // RAW_SLOTS, (r + 2) % RAW_SLOTS, True)
                if more >= 1:
                    split_wo(t + 1, (r + 1) % RAW_SLOTS, not (start and r == 0))

            def copy_out(number, dst):
                sc.wait_ge(down_done, number * CHUNKS + CHUNKS)
                for m in range(MC // 2):
                    last_ = nc.scalar.copy(dst[:, m, :], ps_out[m][:, :])
                last_.then_inc(out_copied_act, 1)

            def group(number, g, first=False, last=False, hooks={}):
                for r in range(RAW_SLOTS):
                    t = number * CHUNKS + g * RAW_SLOTS + r
                    chunk(t, number * GROUPS + g, r, start=first and r < 2,
                          more=min(2, RAW_SLOTS - 1 - r) if last else 2)
                    if r in hooks:
                        hooks[r]()

            def exponentials(b):
                sc.wait_ge(logits_shifted, b + 1)
                nc.scalar.activation(gate_exp[:, :], logit_diff[:, :], ACT.Exp, accum_out=gate_den[:, :]
                                     ).then_inc(exp_done, 1)

            def expert(b, slot, first=False, last=False):
                group(b * 2, 0, first, hooks={} if first else {0: lambda: copy_out(b * 2 - 1, s_out)})
                group(b * 2, 1, hooks={} if first else {2: lambda: exponentials(b - 1)})
                with sc.Fori(2, GROUPS) as g:
                    group(b * 2, g)

            def shared_(b, slot, last=False):
                group(b * 2 + 1, 0, hooks={0: lambda: copy_out(b * 2, e_out)})
                if not last:
                    split_x(b + 1, 1 - slot)
                with sc.Fori(1, GROUPS - 1) as g:
                    group(b * 2 + 1, g)
                group(b * 2 + 1, GROUPS - 1, last=last)

            split_x(0, 0)
            split_wi(0, 0, 0, False)
            split_wi(1, 0, 1, False)
            split_wo(0, 0, False)
            schedule(sc, expert, shared_)
            copy_out(2 * BATCH - 1, s_out)
            exponentials(BATCH - 1)

        @block.vector
        def _(dve):
            def split_x(b, slot):
                dve.wait_ge(x_hi_done, b + 1)
                nc.vector.tensor_tensor(xs[slot][LO][:, :, :], x_raw[:, :, :], xs[slot][HI][:, :, :].bitcast(F32),
                                        ALU.subtract).then_inc(x_ready, 1)

            def split_wi(t, r):
                dve.wait_ge(wi_hi_done, t + 1)
                flat = [wi[r % 2][p][:, :, :, :].rearrange("p a k f -> p (a k f)") for p in (HI, LO)]
                nc.vector.tensor_tensor(flat[LO], raw[r][:, 0:WI], flat[HI].bitcast(F32),
                                        ALU.subtract).then_inc(wi_ready, 1)

            def split_wo(t, r):
                dve.wait_ge(wo_hi_done, t + 1)
                nc.vector.tensor_tensor(wo[r % 2][LO][:, :], raw[r][:, WI:CHUNK_W], wo[r % 2][HI][:, :].bitcast(F32),
                                        ALU.subtract).then_inc(wo_ready, 1)

            def chunk(t, r, start=False, more=2):
                s = r % 2
                dve.wait_ge(lin_projected, t + 1)
                dve.wait_ge(gelu_done, t + 1)
                nc.vector.tensor_tensor(hid[s][:, :], act[s][:, :], ps_lin[s][:, :], ALU.mult
                                        ).then_inc(product_done, 1)
                dve.wait_ge(hid_hi_done, t + 1)
                nc.vector.tensor_tensor(hs[s][LO][:, :], hid[s][:, :], hs[s][HI][:, :].bitcast(F32), ALU.subtract
                                        ).then_inc(hid_ready, 1)
                if more >= 2:
                    split_wi(t + 2, (r + 2) % RAW_SLOTS)
                if more >= 1:
                    split_wo(t + 1, (r + 1) % RAW_SLOTS)

            def copy_out(number, dst):
                dve.wait_ge(down_done, number * CHUNKS + CHUNKS)
                for m in range(MC // 2, MC):
                    last_ = nc.vector.tensor_copy(dst[:, m, :], ps_out[m][:, :])
                last_.then_inc(out_copied_dve, 1)

            def group(number, g, first=False, last=False, hooks={}):
                for r in range(RAW_SLOTS):
                    chunk(number * CHUNKS + g * RAW_SLOTS + r, r, first and r < 2,
                          more=min(2, RAW_SLOTS - 1 - r) if last else 2)
                    if r in hooks:
                        hooks[r]()

            def gate_expert(b):
                dve.wait_ge(row_spread, b * 2 + 1)
                for c in range(NC):
                    last_ = nc.vector.tensor_tensor_reduce(gate_prod[:, c, :], g0_sb[:, c, 0, :], gate_row[:, 0, :], 1.0, 0.0,
                                                           ALU.mult, ALU.add, gate_sum[:, 0, c:c + 1])
                last_.then_inc(gate_step, 1)

            def gate_shared(b):
                dve.wait_ge(row_spread, b * 2 + 2)
                dve.wait_ge(gate_step, b * 3 + 1)
                for c in range(NC):
                    last_ = nc.vector.tensor_tensor_reduce(gate_prod[:, c, :], g0_sb[:, c, 1, :], gate_row[:, 1, :], 1.0,
                                                           gate_sum[:, 0, c:c + 1], ALU.mult, ALU.add,
                                                           gate_sum[:, 1, c:c + 1])
                last_.then_inc(gate_step, 1)
                dve.wait_ge(gate_step, b * 3 + 2)
                nc.vector.tensor_scalar(gate_act[:, :], gate_sum[:, 1, :], 0.0, None, ALU.max).then_inc(gate_step, 1)
                dve.wait_ge(gate_step, b * 3 + 3)
                for c in range(2):
                    nc.vector.tensor_tensor_reduce(logit_prod[:, c, :], g1_sb[:, c, :], gate_act[:, :], 1.0, 0.0, ALU.mult,
                                                   ALU.add, logit_part[:, c:c + 1]).then_inc(logits_part_done, 1)

            def shift_logits(b):
                dve.wait_ge(logits_done, b + 1)
                nc.vector.tensor_reduce(logit_max[:, :], logits[:, :], AX.X, ALU.max).then_inc(max_done, 1)
                dve.wait_ge(max_done, b + 1)
                nc.vector.tensor_scalar(logit_diff[:, :], logits[:, :], logit_max[:, 0:1], None, ALU.subtract
                                        ).then_inc(logits_shifted, 1)

            def combine(b):
                dve.wait_ge(exp_done, b + 1)
                nc.vector.reciprocal(gate_inv[:, :], gate_den[:, :]).then_inc(weight_step, 1)
                dve.wait_ge(weight_step, b * 2 + 1)
                nc.vector.tensor_scalar(gate_w[:, :], gate_exp[:, :], gate_inv[:, 0:1], None, ALU.mult
                                        ).then_inc(weight_step, 1)
                dve.wait_ge(weight_step, b * 2 + 2)
                dve.wait_ge(x_res_loaded, b * 16 + 16)
                dve.wait_ge(out_copied_act, b * 2 + 2)
                nc.vector.scalar_tensor_tensor(mix[:, :, :], e_out[:, :, :], gate_w[:, 0:1], x_res[:, :, :],
                                               ALU.mult, ALU.add).then_inc(mixed, 1)
                dve.wait_ge(mixed, b * 2 + 1)
                nc.vector.scalar_tensor_tensor(mix[:, :, :], s_out[:, :, :], gate_w[:, 1:2], mix[:, :, :],
                                               ALU.mult, ALU.add).then_inc(mixed, 1)

            def expert(b, slot, first=False, last=False):
                group(b * 2, 0, first, hooks={} if first else {0: lambda: copy_out(b * 2 - 1, s_out),
                                                               3: lambda: gate_shared(b - 1)})
                group(b * 2, 1, hooks={} if first else {1: lambda: shift_logits(b - 1)})
                if not first:
                    combine(b - 1)
                with dve.Fori(2, GROUPS) as g:
                    group(b * 2, g)

            def shared_(b, slot, last=False):
                group(b * 2 + 1, 0, hooks={0: lambda: copy_out(b * 2, e_out)})
                if not last:
                    split_x(b + 1, 1 - slot)
                group(b * 2 + 1, 1)
                gate_expert(b)
                with dve.Fori(2, GROUPS - 1) as g:
                    group(b * 2 + 1, g)
                group(b * 2 + 1, GROUPS - 1, last=last)

            dve.wait_ge(gate_weights_loaded, 32)
            split_x(0, 0)
            split_wi(0, 0)
            split_wi(1, 1)
            split_wo(0, 0)
            schedule(dve, expert, shared_)
            copy_out(2 * BATCH - 1, s_out)
            gate_shared(BATCH - 1)
            shift_logits(BATCH - 1)
            combine(BATCH - 1)

        @block.gpsimd
        def _(pool):
            for b in range(BATCH):
                for n, net_out in enumerate((e_out, s_out)):
                    pool.wait_ge(out_copied_act, b * 2 + (n + 1))
                    nc.gpsimd.partition_broadcast(gate_row[:, n, :], net_out[0:1, 0, :]).then_inc(row_spread, 1)
                pool.wait_ge(logits_part_done, b * 2 + 2)
                nc.gpsimd.partition_all_reduce(logits[:, :], logit_part[:, :], P, RADD).then_inc(logits_done, 1)


def kernel(x, itok_B_0_2, L0_cond_Wi0, L0_cond_Wi1, L0_cond_Wo, L0_cond_sWi0, L0_cond_sWi1, L0_cond_sWo,
           L0_cond_g0, L0_cond_g1):
    import numpy as np
    import concourse.bacc as bacc
    from concourse import mybir as mb
    from concourse.bass_utils import run_bass_kernel_spmd

    x, labels = np.asarray(x), np.asarray(itok_B_0_2)
    BATCH, TOK, D = x.shape
    E, _, F = L0_cond_Wi0.shape
    KC, MC, CHUNKS, NC = D // P, TOK // P, F // P, D // P

    def chunked(wi0, wi1, wo):
        n = wi0.shape[0]
        ups = [np.asarray(w).reshape(n, KC, P, CHUNKS, P).transpose(0, 3, 2, 1, 4).reshape(n, CHUNKS, P, D)
               for w in (wi0, wi1)]
        return np.ascontiguousarray(np.concatenate(ups + [np.asarray(wo).reshape(n, CHUNKS, P, D)], axis=-1))

    by_row = x.reshape(BATCH, P, MC, D)
    arrays = {
        "x_cols": by_row.reshape(BATCH, P, MC, KC, P).transpose(0, 4, 3, 2, 1).reshape(BATCH, P, KC, TOK),
        "x_rows": by_row,
        "labels": labels.reshape(1, BATCH),
        "experts": chunked(L0_cond_Wi0, L0_cond_Wi1, L0_cond_Wo),
        "shared": chunked(*(np.asarray(w)[None] for w in (L0_cond_sWi0, L0_cond_sWi1, L0_cond_sWo)))[0],
        "g0_rows": np.asarray(L0_cond_g0).reshape(2, D, NC, P).transpose(3, 2, 0, 1),
        "g1_rows": np.asarray(L0_cond_g1).reshape(NC, P, 2).transpose(1, 2, 0),
    }
    arrays = {name: np.ascontiguousarray(a) for name, a in arrays.items()}

    nc = bacc.Bacc("TRN2", target_bir_lowering=False, num_devices=1)
    args = [nc.dram_tensor(name, a.shape, mb.dt.from_np(a.dtype), kind="ExternalInput").ap()
            for name, a in arrays.items()]
    out = nc.dram_tensor("out", by_row.shape, mb.dt.from_np(x.dtype), kind="ExternalOutput").ap()
    build(nc, *args, out)
    results = run_bass_kernel_spmd(nc, [arrays], core_ids=[0])
    return results.results[0]["out"].reshape(x.shape)
```

```python
from contextlib import ExitStack

import concourse.bass as bass
from concourse import mybir

F32 = mybir.dt.float32
F32R = mybir.dt.float32r
I32 = mybir.dt.int32
ALU = mybir.AluOpType
ACT = mybir.ActivationFunctionType
AX = mybir.AxisListType
RADD = bass.bass_isa.ReduceOp.add

P = 128
RAW_SLOTS = 4
IDLE_MATMULS = 9
HI, LO = 0, 1
EXPERT, SHARED = 0, 1
PASSES = [(LO, HI), (HI, LO), (HI, HI)]


def build(nc, x_cols, x_rows, labels, experts, shared, g0_rows, g1_rows, out):
    BATCH, _, KC, TOK = x_cols.shape
    N_EXPERTS, CHUNKS, _, CHUNK_W = experts.shape
    D = KC * P
    MC = TOK // P
    WI = 2 * D
    WO = D
    NC = g0_rows.shape[1]
    assert CHUNK_W == WI + WO and CHUNKS % RAW_SLOTS == 0 and BATCH % 2 == 0
    GROUPS = CHUNKS // RAW_SLOTS
    PAIRS = BATCH // 2

    with ExitStack() as ctx:
        def sb(name, shape, dt=F32):
            return ctx.enter_context(nc.sbuf_tensor(name, shape, dt))

        def sem(name):
            return ctx.enter_context(nc.semaphore(name))

        raw = [sb(f"raw{r}", [P, CHUNK_W]) for r in range(RAW_SLOTS)]
        wi = [[sb(f"wi{s}{p}", [P, 2, KC, P], F32R) for p in "hl"] for s in range(2)]
        wo = [[sb(f"wo{s}{p}", [P, D], F32R) for p in "hl"] for s in range(2)]
        x_raw = sb("x_raw", [P, KC, TOK])
        xs = [[sb(f"x{s}{p}", [P, KC, TOK], F32R) for p in "hl"] for s in range(2)]
        act = [sb(f"act{s}", [P, TOK]) for s in range(2)]
        hid = [sb(f"hid{s}", [P, TOK]) for s in range(2)]
        hs = [[sb(f"hid{s}{p}", [P, TOK], F32R) for p in "hl"] for s in range(2)]
        s_out = sb("s_out", [P, MC, D])
        e_out = sb("e_out", [P, MC, D])
        x_res = sb("x_res", [P, MC, D])
        mix = sb("mix", [P, MC, D])
        g0_sb = sb("g0_sb", [P, NC, 2, D])
        g1_sb = sb("g1_sb", [P, 2, NC])
        gate_row = sb("gate_row", [P, 2, D])
        gate_prod = sb("gate_prod", [P, NC, D])
        gate_sum = sb("gate_sum", [P, 2, NC])
        gate_act = sb("gate_act", [P, NC])
        logit_prod = sb("logit_prod", [P, 2, NC])
        logit_part = sb("logit_part", [P, 2])
        logits = sb("logits", [P, 2])
        logit_max = sb("logit_max", [P, 1])
        logit_diff = sb("logit_diff", [P, 2])
        exp_warm = sb("exp_warm", [P, 1])
        gate_exp = sb("gate_exp", [P, 2])
        gate_den = sb("gate_den", [P, 1])
        gate_inv = sb("gate_inv", [P, 1])
        gate_w = sb("gate_w", [P, 2])
        idle = sb("idle", [P, D], mybir.dt.bfloat16)
        labels_sb = sb("labels_sb", [1, BATCH], I32)

        def bank(name):
            return ctx.enter_context(nc.psum_tensor(name, [P, 512], F32))

        ps_gate = [bank(f"ps_gate{s}") for s in range(2)]
        ps_lin = [bank(f"ps_lin{s}") for s in range(2)]
        ps_out = [bank(f"ps_out{m}") for m in range(MC)]

        raw_loaded = [sem(f"raw_loaded{r}") for r in range(RAW_SLOTS)]
        idle_ready = sem("idle_ready")
        labels_loaded = sem("labels_loaded")
        gate_weights_loaded = sem("gate_weights_loaded")
        x_raw_loaded = [sem(f"x_raw_loaded{k}") for k in range(KC)]
        x_res_loaded = sem("x_res_loaded")
        out_stored = sem("out_stored")
        x_hi_done = sem("x_hi_done")
        x_ready = sem("x_ready")
        first_loaded = [sem(f"first_loaded{w}") for w in range(2)]
        first_hi_done = sem("first_hi_done")
        first_ready = sem("first_ready")
        wi_hi_done = sem("wi_hi_done")
        wi_ready = sem("wi_ready")
        wo_hi_done = sem("wo_hi_done")
        wo_ready = sem("wo_ready")
        gate_projected = sem("gate_projected")
        lin_projected = sem("lin_projected")
        gelu_done = sem("gelu_done")
        product_done = sem("product_done")
        hid_hi_done = sem("hid_hi_done")
        hid_ready = sem("hid_ready")
        down_done = sem("down_done")
        out_copied_act = sem("out_copied_act")
        out_copied_dve = sem("out_copied_dve")
        row_spread = sem("row_spread")
        gate_step = sem("gate_step")
        logits_part_done = sem("logits_part_done")
        logits_done = sem("logits_done")
        logits_shifted = sem("logits_shifted")
        max_done = sem("max_done")
        exp_done = sem("exp_done")
        weight_step = sem("weight_step")
        mixed = sem("mixed")
        last_down_done = sem("last_down_done")
        last_scaled_s = sem("last_scaled_s")
        last_scaled_e = sem("last_scaled_e")
        last_mixed = sem("last_mixed")
        last_mixed_dve = sem("last_mixed_dve")

        block = ctx.enter_context(nc.Block())

        def schedule(eng, shared_pass, expert_pass):
            shared_pass(0, 0, first=True)
            with eng.Fori(0, PAIRS - 1) as i:
                expert_pass(i * 2, 0)
                shared_pass(i * 2 + 1, 1)
                expert_pass(i * 2 + 1, 1)
                shared_pass(i * 2 + 2, 0)
            expert_pass(BATCH - 2, 0)
            shared_pass(BATCH - 1, 1, last=True)
            expert_pass(BATCH - 1, 1, last=True)

        @block.sync
        def _(sp):
            def load_pass(weights, t0, first, between):
                def group(g, wait):
                    for r in range(RAW_SLOTS):
                        if not wait and r == 0:
                            for w in range(2):
                                sp.dma_start(raw[0][:, w * D:(w + 1) * D], weights(0)[:, w * D:(w + 1) * D]
                                             ).then_inc(first_loaded[w], 16)
                                if w == 0:
                                    for k in range(KC):
                                        sp.dma_start(x_raw[:, k, :], x_cols[0, :, k, :]).then_inc(x_raw_loaded[k], 16)
                            sp.dma_start(raw[0][:, WI:CHUNK_W], weights(0)[:, WI:CHUNK_W]).then_inc(raw_loaded[0], 16)
                            continue
                        if wait:
                            sp.wait_ge(wo_ready, t0 + g * RAW_SLOTS + (r + 1 - RAW_SLOTS))
                        sp.dma_start(raw[r][:, :], weights(g * RAW_SLOTS + r)).then_inc(raw_loaded[r], 16)

                group(0, not first)
                between()
                with sp.Fori(1, GROUPS) as g:
                    group(g, True)

            def shared_pass(b, slot, first=False, last=False):
                def next_x():
                    sp.wait_ge(x_ready, (b + 1) * KC)
                    rows = x_cols[bass.ds(b + 1, 1)].rearrange("b p k s -> (b p) k s")
                    for k in range(KC):
                        sp.dma_start(x_raw[:, k, :], rows[:, k, :]).then_inc(x_raw_loaded[k], 16)

                load_pass(lambda c: shared[bass.ds(c, 1)].rearrange("c p w -> (c p) w"),
                          b * (2 * CHUNKS), first, (lambda: None) if last else next_x)
                if not first:
                    store(b - 1)
                    sp.wait_ge(out_stored, b * 16)
                else:
                    sp.dma_start(labels_sb[:, :], labels).then_inc(labels_loaded, 16)
                    sp.dma_start(g0_sb[:, :, :, :], g0_rows).then_inc(gate_weights_loaded, 16)
                    sp.dma_start(g1_sb[:, :, :], g1_rows).then_inc(gate_weights_loaded, 16)
                sp.dma_start(x_res[:, :, :], x_rows[bass.ds(b, 1)].rearrange("b p m d -> (b p) m d")
                             ).then_inc(x_res_loaded, 16)

            def expert_pass(b, slot, last=False):
                sp.wait_ge(labels_loaded, 16)
                label = sp.value_load(labels_sb[0:1, bass.ds(b, 1)], min_val=0, max_val=N_EXPERTS - 1)
                load_pass(lambda c: experts[bass.ds(label, 1), bass.ds(c, 1)].rearrange("e c p w -> (e c p) w"),
                          b * (2 * CHUNKS) + CHUNKS, False, lambda: None)

            def store(b):
                sp.wait_ge(mixed, b * 2 + 2)
                sp.dma_start(out[bass.ds(b, 1)].rearrange("b p m d -> (b p) m d"), mix[:, :, :]
                             ).then_inc(out_stored, 16)

            schedule(sp, shared_pass, expert_pass)
            for m in range(MC):
                if m < MC // 2:
                    sp.wait_ge(last_mixed, m + 1)
                else:
                    sp.wait_ge(last_mixed_dve, m + 1 - MC // 2)
                sp.dma_start(out[BATCH - 1, :, m, :], mix[:, m, :]).then_inc(out_stored, 16)
            sp.wait_ge(out_stored, 16 * (BATCH - 1 + MC))

        @block.tensor
        def _(pe):
            def project(t, s, xslot, number=None):
                if number != 0:
                    pe.wait_ge(wi_ready, t)
                for which, bank_, free, done in ((0, ps_gate[s], gelu_done, gate_projected),
                                                 (1, ps_lin[s], product_done, lin_projected)):
                    if number == 0:
                        pe.wait_ge(first_ready, which + 1)
                    elif number != 1:
                        pe.wait_ge(free, t - 1)
                    for k in range(KC):
                        if number == 0:
                            pe.wait_ge(x_ready, k + 1)
                        for n, (wp, xp) in enumerate(PASSES):
                            mm = nc.tensor.matmul(bank_[:, :], wi[s][wp][:, which, k, :], xs[xslot][xp][:, k, :],
                                                  start=(n == 0 and k == 0), stop=(n == 2 and k == KC - 1))
                    mm.then_inc(done, 1)

            def back(t, s, start=False, stop=False, last=False):
                pe.wait_ge(hid_ready, t + 1)
                pe.wait_ge(wo_ready, t + 1)
                for m in range(MC):
                    for n, (hp, wp) in enumerate(PASSES):
                        mm = nc.tensor.matmul(ps_out[m][:, :], hs[s][hp][:, m * P:(m + 1) * P], wo[s][wp][:, :],
                                              start=(start and n == 0), stop=(stop and n == 2),
                                              skip_group_check=True)
                    if last:
                        mm.then_inc(last_down_done, 1)
                if not last:
                    mm.then_inc(down_done, 1)

            def run_pass(number, xslot, next_xslot, next_batch, first=False, last=False):
                t0 = number * CHUNKS
                project(t0 + 1, 1, xslot, 1 if first else None)
                if not first:
                    pe.wait_ge(out_copied_act, number)
                    pe.wait_ge(out_copied_dve, number)
                back(t0, 0, start=True)
                with pe.Fori(1, CHUNKS // 2) as j:
                    project(t0 + j * 2, 0, xslot)
                    back(t0 + j * 2 - 1, 1)
                    project(t0 + j * 2 + 1, 1, xslot)
                    back(t0 + j * 2, 0)
                if not last:
                    if next_batch is not None:
                        pe.wait_ge(x_ready, (next_batch + 1) * KC)
                    project(t0 + CHUNKS, 0, next_xslot)
                back(t0 + CHUNKS - 1, 1, stop=True, last=last)

            def shared_pass(b, slot, first=False, last=False):
                run_pass(b * 2, slot, slot, None, first)

            def expert_pass(b, slot, last=False):
                run_pass(b * 2 + 1, slot, 1 - slot, b + 1, last=last)

            pe.wait_ge(idle_ready, 1)
            for _ in range(IDLE_MATMULS):
                nc.tensor.matmul(ps_out[0][:, :], idle[:, 0:P], idle[:, :], start=True, stop=True)
            project(0, 0, 0, number=0)
            schedule(pe, shared_pass, expert_pass)

        @block.scalar
        def _(sc):
            def split_x(b, slot):
                for k in range(KC):
                    sc.wait_ge(x_raw_loaded[k], b * 16 + 16)
                    nc.scalar.copy(xs[slot][HI][:, k, :], x_raw[:, k, :]).then_inc(x_hi_done, 1)

            def split_wi(t, lap, r, free):
                sc.wait_ge(raw_loaded[r], lap * 16 + 16)
                if free:
                    sc.wait_ge(lin_projected, t - 1)
                nc.scalar.copy(wi[r % 2][HI][:, :, :, :].rearrange("p a k f -> p (a k f)"), raw[r][:, 0:WI]
                               ).then_inc(wi_hi_done, 1)

            def split_wo(t, r, free):
                if free:
                    sc.wait_ge(down_done, t - 1)
                nc.scalar.copy(wo[r % 2][HI][:, :], raw[r][:, WI:CHUNK_W]).then_inc(wo_hi_done, 1)

            def chunk(t, lap, r, start=False, more=2):
                s = r % 2
                sc.wait_ge(gate_projected, t + 1)
                if not start:
                    sc.wait_ge(product_done, t - 1)
                nc.scalar.activation(act[s][:, :], ps_gate[s][:, :], ACT.Gelu_apprx_tanh).then_inc(gelu_done, 1)
                sc.wait_ge(product_done, t + 1)
                if not start:
                    sc.wait_ge(down_done, t - 1)
                nc.scalar.copy(hs[s][HI][:, :], hid[s][:, :]).then_inc(hid_hi_done, 1)
                if more >= 2:
                    split_wi(t + 2, lap + (r + 2) // RAW_SLOTS, (r + 2) % RAW_SLOTS, True)
                if more >= 1:
                    split_wo(t + 1, (r + 1) % RAW_SLOTS, not (start and r == 0))

            def copy_out(number, dst):
                sc.wait_ge(down_done, number * CHUNKS + CHUNKS)
                for m in range(MC // 2):
                    last_ = nc.scalar.copy(dst[:, m, :], ps_out[m][:, :])
                last_.then_inc(out_copied_act, 1)

            def group(number, g, first=False, last=False, hooks={}):
                for r in range(RAW_SLOTS):
                    t = number * CHUNKS + g * RAW_SLOTS + r
                    chunk(t, number * GROUPS + g, r, start=first and r < 2,
                          more=min(2, RAW_SLOTS - 1 - r) if last else 2)
                    if r in hooks:
                        hooks[r]()

            def exponentials(b):
                sc.wait_ge(logits_shifted, b + 1)
                nc.scalar.activation(gate_exp[:, :], logit_diff[:, :], ACT.Exp, accum_out=gate_den[:, :]
                                     ).then_inc(exp_done, 1)

            def shared_pass(b, slot, first=False, last=False):
                group(b * 2, 0, first, hooks={} if first else {0: lambda: copy_out(b * 2 - 1, e_out)})
                group(b * 2, 1, hooks={} if first else {2: lambda: exponentials(b - 1)})
                with sc.Fori(2, GROUPS) as g:
                    group(b * 2, g)

            def expert_pass(b, slot, last=False):
                group(b * 2 + 1, 0, hooks={0: lambda: copy_out(b * 2, s_out)})
                if not last:
                    split_x(b + 1, 1 - slot)
                with sc.Fori(1, GROUPS - 1) as g:
                    group(b * 2 + 1, g)
                group(b * 2 + 1, GROUPS - 1, last=last)

            for w in range(2):
                sc.wait_ge(first_loaded[w], 16)
                nc.scalar.copy(wi[0][HI][:, w, :, :], raw[0][:, w * D:(w + 1) * D].rearrange("p (k f) -> p k f", k=KC)
                               ).then_inc(first_hi_done, 1)
                if w == 0:
                    split_x(0, 0)
            split_wi(1, 0, 1, False)
            sc.wait_ge(raw_loaded[0], 16)
            split_wo(0, 0, False)
            schedule(sc, shared_pass, expert_pass)
            nc.scalar.activation(exp_warm[:, :], logits[:, 0:1], ACT.Exp)
            sc.wait_ge(last_down_done, 1)
            nc.scalar.copy(e_out[0:1, 0, :], ps_out[0][0:1, :]).then_inc(out_copied_act, 1)
            exponentials(BATCH - 1)
            sc.wait_ge(weight_step, BATCH * 2)
            for m in range(MC):
                nc.scalar.activation(s_out[:, m, :], s_out[:, m, :], ACT.Copy, scale=gate_w[:, SHARED:SHARED + 1]
                                     ).then_inc(last_scaled_s, 1)

        @block.vector
        def _(dve):
            def split_x(b, slot):
                for k in range(KC):
                    dve.wait_ge(x_hi_done, b * KC + (k + 1))
                    nc.vector.tensor_tensor(xs[slot][LO][:, k, :], x_raw[:, k, :], xs[slot][HI][:, k, :].bitcast(F32),
                                            ALU.subtract).then_inc(x_ready, 1)

            def split_wi(t, r):
                dve.wait_ge(wi_hi_done, t)
                flat = [wi[r % 2][p][:, :, :, :].rearrange("p a k f -> p (a k f)") for p in (HI, LO)]
                nc.vector.tensor_tensor(flat[LO], raw[r][:, 0:WI], flat[HI].bitcast(F32),
                                        ALU.subtract).then_inc(wi_ready, 1)

            def split_wo(t, r):
                dve.wait_ge(wo_hi_done, t + 1)
                nc.vector.tensor_tensor(wo[r % 2][LO][:, :], raw[r][:, WI:CHUNK_W], wo[r % 2][HI][:, :].bitcast(F32),
                                        ALU.subtract).then_inc(wo_ready, 1)

            def chunk(t, r, start=False, more=2):
                s = r % 2
                dve.wait_ge(lin_projected, t + 1)
                dve.wait_ge(gelu_done, t + 1)
                nc.vector.tensor_tensor(hid[s][:, :], act[s][:, :], ps_lin[s][:, :], ALU.mult
                                        ).then_inc(product_done, 1)
                dve.wait_ge(hid_hi_done, t + 1)
                nc.vector.tensor_tensor(hs[s][LO][:, :], hid[s][:, :], hs[s][HI][:, :].bitcast(F32), ALU.subtract
                                        ).then_inc(hid_ready, 1)
                if more >= 2:
                    split_wi(t + 2, (r + 2) % RAW_SLOTS)
                if more >= 1:
                    split_wo(t + 1, (r + 1) % RAW_SLOTS)

            def copy_out(number, dst):
                dve.wait_ge(down_done, number * CHUNKS + CHUNKS)
                for m in range(MC // 2, MC):
                    last_ = nc.vector.tensor_copy(dst[:, m, :], ps_out[m][:, :])
                last_.then_inc(out_copied_dve, 1)

            def group(number, g, first=False, last=False, hooks={}):
                for r in range(RAW_SLOTS):
                    chunk(number * CHUNKS + g * RAW_SLOTS + r, r, first and r < 2,
                          more=min(2, RAW_SLOTS - 1 - r) if last else 2)
                    if r in hooks:
                        hooks[r]()

            def gate_shared(b):
                dve.wait_ge(gate_weights_loaded, 32)
                dve.wait_ge(row_spread, b * 2 + 1)
                for c in range(NC):
                    last_ = nc.vector.tensor_tensor_reduce(gate_prod[:, c, :], g0_sb[:, c, SHARED, :], gate_row[:, 0, :],
                                                           1.0, 0.0, ALU.mult, ALU.add, gate_sum[:, 0, c:c + 1])
                last_.then_inc(gate_step, 1)

            def gate_expert(b):
                dve.wait_ge(row_spread, b * 2 + 2)
                dve.wait_ge(gate_step, b * 3 + 1)
                for c in range(NC):
                    last_ = nc.vector.tensor_tensor_reduce(gate_prod[:, c, :], g0_sb[:, c, EXPERT, :], gate_row[:, 1, :],
                                                           1.0, gate_sum[:, 0, c:c + 1], ALU.mult, ALU.add,
                                                           gate_sum[:, 1, c:c + 1])
                last_.then_inc(gate_step, 1)
                dve.wait_ge(gate_step, b * 3 + 2)
                nc.vector.tensor_scalar(gate_act[:, :], gate_sum[:, 1, :], 0.0, None, ALU.max).then_inc(gate_step, 1)
                dve.wait_ge(gate_step, b * 3 + 3)
                for c in range(2):
                    nc.vector.tensor_tensor_reduce(logit_prod[:, c, :], g1_sb[:, c, :], gate_act[:, :], 1.0, 0.0,
                                                   ALU.mult, ALU.add, logit_part[:, c:c + 1]
                                                   ).then_inc(logits_part_done, 1)

            def shift_logits(b):
                dve.wait_ge(logits_done, b + 1)
                nc.vector.tensor_reduce(logit_max[:, :], logits[:, :], AX.X, ALU.max).then_inc(max_done, 1)
                dve.wait_ge(max_done, b + 1)
                nc.vector.tensor_scalar(logit_diff[:, :], logits[:, :], logit_max[:, 0:1], None, ALU.subtract
                                        ).then_inc(logits_shifted, 1)

            def gate_weights(b):
                dve.wait_ge(exp_done, b + 1)
                nc.vector.reciprocal(gate_inv[:, :], gate_den[:, :]).then_inc(weight_step, 1)
                dve.wait_ge(weight_step, b * 2 + 1)
                nc.vector.tensor_scalar(gate_w[:, :], gate_exp[:, :], gate_inv[:, 0:1], None, ALU.mult
                                        ).then_inc(weight_step, 1)

            def combine(b):
                dve.wait_ge(weight_step, b * 2 + 2)
                dve.wait_ge(x_res_loaded, b * 16 + 16)
                dve.wait_ge(out_copied_act, b * 2 + 2)
                nc.vector.scalar_tensor_tensor(mix[:, :, :], s_out[:, :, :], gate_w[:, SHARED:SHARED + 1], x_res[:, :, :],
                                               ALU.mult, ALU.add).then_inc(mixed, 1)
                dve.wait_ge(mixed, b * 2 + 1)
                nc.vector.scalar_tensor_tensor(mix[:, :, :], e_out[:, :, :], gate_w[:, EXPERT:EXPERT + 1], mix[:, :, :],
                                               ALU.mult, ALU.add).then_inc(mixed, 1)

            def shared_pass(b, slot, first=False, last=False):
                group(b * 2, 0, first, hooks={} if first else {0: lambda: copy_out(b * 2 - 1, e_out),
                                                               3: lambda: gate_expert(b - 1)})
                group(b * 2, 1, hooks={} if first else {1: lambda: shift_logits(b - 1)})
                if not first:
                    gate_weights(b - 1)
                    combine(b - 1)
                with dve.Fori(2, GROUPS) as g:
                    group(b * 2, g)

            def expert_pass(b, slot, last=False):
                group(b * 2 + 1, 0, hooks={0: lambda: copy_out(b * 2, s_out)})
                if not last:
                    split_x(b + 1, 1 - slot)
                group(b * 2 + 1, 1)
                gate_shared(b)
                with dve.Fori(2, GROUPS - 1) as g:
                    group(b * 2 + 1, g)
                group(b * 2 + 1, GROUPS - 1, last=last)

            nc.vector.memset(idle[:, :], 0.0).then_inc(idle_ready, 1)
            for w in range(2):
                dve.wait_ge(first_hi_done, w + 1)
                part = raw[0][:, w * D:(w + 1) * D].rearrange("p (k f) -> p k f", k=KC)
                nc.vector.tensor_tensor(wi[0][LO][:, w, :, :], part, wi[0][HI][:, w, :, :].bitcast(F32), ALU.subtract
                                        ).then_inc(first_ready, 1)
                if w == 0:
                    split_x(0, 0)
            split_wi(1, 1)
            split_wo(0, 0)
            schedule(dve, shared_pass, expert_pass)
            gate_expert(BATCH - 1)
            shift_logits(BATCH - 1)
            gate_weights(BATCH - 1)
            dve.wait_ge(weight_step, BATCH * 2)
            dve.wait_ge(x_res_loaded, BATCH * 16)
            for m in range(MC):
                dve.wait_ge(last_down_done, m + 1)
                nc.vector.scalar_tensor_tensor(e_out[:, m, :], ps_out[m][:, :], gate_w[:, EXPERT:EXPERT + 1],
                                               x_res[:, m, :], ALU.mult, ALU.add).then_inc(last_scaled_e, 1)
            for m in range(MC // 2, MC):
                dve.wait_ge(last_scaled_s, m + 1)
                dve.wait_ge(last_scaled_e, m + 1)
                nc.vector.tensor_tensor(mix[:, m, :], e_out[:, m, :], s_out[:, m, :], ALU.add).then_inc(last_mixed_dve, 1)

        @block.gpsimd
        def _(pool):
            for b in range(BATCH):
                for n, net_out in enumerate((s_out, e_out)):
                    pool.wait_ge(out_copied_act, b * 2 + (n + 1))
                    nc.gpsimd.partition_broadcast(gate_row[:, n, :], net_out[0:1, 0, :]).then_inc(row_spread, 1)
                pool.wait_ge(logits_part_done, b * 2 + 2)
                nc.gpsimd.partition_all_reduce(logits[:, :], logit_part[:, :], P, RADD).then_inc(logits_done, 1)
            for m in range(MC // 2):
                pool.wait_ge(last_scaled_s, m + 1)
                pool.wait_ge(last_scaled_e, m + 1)
                nc.gpsimd.tensor_tensor(mix[:, m, :], e_out[:, m, :], s_out[:, m, :], ALU.add).then_inc(last_mixed, 1)


def kernel(x, itok_B_0_2, L0_cond_Wi0, L0_cond_Wi1, L0_cond_Wo, L0_cond_sWi0, L0_cond_sWi1, L0_cond_sWo,
           L0_cond_g0, L0_cond_g1):
    import numpy as np
    import concourse.bacc as bacc
    from concourse import mybir as mb
    from concourse.bass_utils import run_bass_kernel_spmd

    x, labels = np.asarray(x), np.asarray(itok_B_0_2)
    BATCH, TOK, D = x.shape
    E, _, F = L0_cond_Wi0.shape
    KC, MC, CHUNKS, NC = D // P, TOK // P, F // P, D // P

    def chunked(wi0, wi1, wo):
        n = wi0.shape[0]
        ups = [np.asarray(w).reshape(n, KC, P, CHUNKS, P).transpose(0, 3, 2, 1, 4).reshape(n, CHUNKS, P, D)
               for w in (wi0, wi1)]
        return np.ascontiguousarray(np.concatenate(ups + [np.asarray(wo).reshape(n, CHUNKS, P, D)], axis=-1))

    by_row = x.reshape(BATCH, P, MC, D)
    arrays = {
        "x_cols": by_row.reshape(BATCH, P, MC, KC, P).transpose(0, 4, 3, 2, 1).reshape(BATCH, P, KC, TOK),
        "x_rows": by_row,
        "labels": labels.reshape(1, BATCH),
        "experts": chunked(L0_cond_Wi0, L0_cond_Wi1, L0_cond_Wo),
        "shared": chunked(*(np.asarray(w)[None] for w in (L0_cond_sWi0, L0_cond_sWi1, L0_cond_sWo)))[0],
        "g0_rows": np.asarray(L0_cond_g0).reshape(2, D, NC, P).transpose(3, 2, 0, 1),
        "g1_rows": np.asarray(L0_cond_g1).reshape(NC, P, 2).transpose(1, 2, 0),
    }
    arrays = {name: np.ascontiguousarray(a) for name, a in arrays.items()}

    nc = bacc.Bacc("TRN2", target_bir_lowering=False, num_devices=1)
    args = [nc.dram_tensor(name, a.shape, mb.dt.from_np(a.dtype), kind="ExternalInput").ap()
            for name, a in arrays.items()]
    out = nc.dram_tensor("out", by_row.shape, mb.dt.from_np(x.dtype), kind="ExternalOutput").ap()
    build(nc, *args, out)
    results = run_bass_kernel_spmd(nc, [arrays], core_ids=[0])
    return results.results[0]["out"].reshape(x.shape)
```

```python
from contextlib import ExitStack

import concourse.bass as bass
from concourse import mybir

F32 = mybir.dt.float32
F32R = mybir.dt.float32r
I32 = mybir.dt.int32
ALU = mybir.AluOpType
ACT = mybir.ActivationFunctionType
AX = mybir.AxisListType
RADD = bass.bass_isa.ReduceOp.add

P = 128
RAW_SLOTS = 4
IDLE_MATMULS = 9
PUT_OFF = 6
BETWEEN = 3
HI, LO = 0, 1
EXPERT, SHARED = 0, 1
PASSES = [(LO, HI), (HI, LO), (HI, HI)]


def build(nc, x_cols, x_rows, labels, experts, shared, g0_rows, g1_rows, out):
    BATCH, _, KC, TOK = x_cols.shape
    N_EXPERTS, CHUNKS, _, CHUNK_W = experts.shape
    D = KC * P
    MC = TOK // P
    WI = 2 * D
    WO = D
    NC = g0_rows.shape[1]
    assert CHUNK_W == WI + WO and CHUNKS % RAW_SLOTS == 0 and BATCH % 2 == 0
    assert PUT_OFF % 2 == 0 and PUT_OFF <= 2 * RAW_SLOTS and BETWEEN < PUT_OFF
    GROUPS = CHUNKS // RAW_SLOTS
    PAIRS = BATCH // 2

    with ExitStack() as ctx:
        def sb(name, shape, dt=F32):
            return ctx.enter_context(nc.sbuf_tensor(name, shape, dt))

        def sem(name):
            return ctx.enter_context(nc.semaphore(name))

        raw = [sb(f"raw{r}", [P, CHUNK_W]) for r in range(RAW_SLOTS)]
        wi = [[sb(f"wi{s}{p}", [P, 2, KC, P], F32R) for p in "hl"] for s in range(2)]
        wo = [[sb(f"wo{s}{p}", [P, D], F32R) for p in "hl"] for s in range(PUT_OFF)]
        x_raw = sb("x_raw", [P, KC, TOK])
        xs = [[sb(f"x{s}{p}", [P, KC, TOK], F32R) for p in "hl"] for s in range(2)]
        act = [sb(f"act{s}", [P, TOK]) for s in range(2)]
        hid = [sb(f"hid{s}", [P, TOK]) for s in range(2)]
        hs = [[sb(f"hid{s}{p}", [P, TOK], F32R) for p in "hl"] for s in range(PUT_OFF)]
        s_out = sb("s_out", [P, MC, D])
        e_out = sb("e_out", [P, MC, D])
        x_res = sb("x_res", [P, MC, D])
        mix = sb("mix", [P, MC, D])
        g0_sb = sb("g0_sb", [P, NC, 2, D])
        g1_sb = sb("g1_sb", [P, 2, NC])
        gate_row = sb("gate_row", [P, 2, D])
        gate_prod = sb("gate_prod", [P, NC, D])
        gate_sum = sb("gate_sum", [P, 2, NC])
        gate_act = sb("gate_act", [P, NC])
        logit_prod = sb("logit_prod", [P, 2, NC])
        logit_part = sb("logit_part", [P, 2])
        logits = sb("logits", [P, 2])
        logit_max = sb("logit_max", [P, 1])
        logit_diff = sb("logit_diff", [P, 2])
        exp_warm = sb("exp_warm", [P, 1])
        gate_exp = sb("gate_exp", [P, 2])
        gate_den = sb("gate_den", [P, 1])
        gate_inv = sb("gate_inv", [P, 1])
        gate_w = sb("gate_w", [P, 2])
        idle = sb("idle", [P, D], mybir.dt.bfloat16)
        labels_sb = sb("labels_sb", [1, BATCH], I32)

        def bank(name):
            return ctx.enter_context(nc.psum_tensor(name, [P, 512], F32))

        ps_gate = [bank(f"ps_gate{s}") for s in range(2)]
        ps_lin = [bank(f"ps_lin{s}") for s in range(2)]
        ps_out = [bank(f"ps_out{m}") for m in range(MC)]

        raw_loaded = [sem(f"raw_loaded{r}") for r in range(RAW_SLOTS)]
        idle_ready = sem("idle_ready")
        labels_loaded = sem("labels_loaded")
        gate_weights_loaded = sem("gate_weights_loaded")
        x_raw_loaded = [sem(f"x_raw_loaded{k}") for k in range(KC)]
        x_res_loaded = sem("x_res_loaded")
        out_stored = sem("out_stored")
        x_hi_done = sem("x_hi_done")
        x_ready = sem("x_ready")
        first_loaded = [sem(f"first_loaded{k}") for k in range(KC)]
        first_hi_done = sem("first_hi_done")
        first_ready = sem("first_ready")
        second_wo_loaded = sem("second_wo_loaded")
        wi_hi_done = sem("wi_hi_done")
        wi_ready = sem("wi_ready")
        wo_hi_done = sem("wo_hi_done")
        wo_ready = sem("wo_ready")
        gate_projected = sem("gate_projected")
        lin_projected = sem("lin_projected")
        gelu_done = sem("gelu_done")
        product_done = sem("product_done")
        hid_hi_done = sem("hid_hi_done")
        hid_ready = sem("hid_ready")
        down_done = sem("down_done")
        out_copied_act = sem("out_copied_act")
        out_copied_dve = sem("out_copied_dve")
        row_spread = sem("row_spread")
        gate_step = sem("gate_step")
        logits_part_done = sem("logits_part_done")
        logits_done = sem("logits_done")
        logits_shifted = sem("logits_shifted")
        max_done = sem("max_done")
        exp_done = sem("exp_done")
        weight_step = sem("weight_step")
        mixed = sem("mixed")
        last_down_done = sem("last_down_done")
        last_scaled = sem("last_scaled")
        last_based_pool = sem("last_based_pool")
        last_based_dve = sem("last_based_dve")
        last_mixed = sem("last_mixed")

        block = ctx.enter_context(nc.Block())

        def back_slot(c, last):
            return c - (CHUNKS - PUT_OFF) if last and c >= CHUNKS - PUT_OFF else c % 2

        def schedule(eng, shared_pass, expert_pass):
            shared_pass(0, 0, first=True)
            with eng.Fori(0, PAIRS - 1) as i:
                expert_pass(i * 2, 0)
                shared_pass(i * 2 + 1, 1)
                expert_pass(i * 2 + 1, 1)
                shared_pass(i * 2 + 2, 0)
            expert_pass(BATCH - 2, 0)
            shared_pass(BATCH - 1, 1, last=True)
            expert_pass(BATCH - 1, 1, last=True)

        @block.sync
        def _(sp):
            def first_group(weights):
                for k in range(KC):
                    sp.dma_start(raw[0][:, 0:WI].rearrange("p (a k f) -> p a k f", a=2, k=KC)[:, :, k, :],
                                 weights(0)[:, 0:WI].rearrange("p (a k f) -> p a k f", a=2, k=KC)[:, :, k, :]
                                 ).then_inc(first_loaded[k], 16)
                    sp.dma_start(x_raw[:, k, :], x_cols[0, :, k, :]).then_inc(x_raw_loaded[k], 16)
                sp.dma_start(raw[1][:, 0:WI], weights(1)[:, 0:WI]).then_inc(raw_loaded[1], 16)
                sp.dma_start(raw[0][:, WI:CHUNK_W], weights(0)[:, WI:CHUNK_W]).then_inc(raw_loaded[0], 16)
                sp.dma_start(raw[1][:, WI:CHUNK_W], weights(1)[:, WI:CHUNK_W]).then_inc(second_wo_loaded, 16)
                for r in range(2, RAW_SLOTS):
                    sp.dma_start(raw[r][:, :], weights(r)).then_inc(raw_loaded[r], 16)

            def load_pass(weights, t0, first, between):
                def group(g):
                    for r in range(RAW_SLOTS):
                        sp.wait_ge(wo_ready, t0 + g * RAW_SLOTS + (r + 1 - RAW_SLOTS))
                        sp.dma_start(raw[r][:, :], weights(g * RAW_SLOTS + r)).then_inc(raw_loaded[r], 16)

                if first:
                    first_group(weights)
                else:
                    group(0)
                between()
                with sp.Fori(1, GROUPS) as g:
                    group(g)

            def shared_pass(b, slot, first=False, last=False):
                def next_x():
                    sp.wait_ge(x_ready, (b + 1) * KC)
                    rows = x_cols[bass.ds(b + 1, 1)].rearrange("b p k s -> (b p) k s")
                    for k in range(KC):
                        sp.dma_start(x_raw[:, k, :], rows[:, k, :]).then_inc(x_raw_loaded[k], 16)

                load_pass(lambda c: shared[bass.ds(c, 1)].rearrange("c p w -> (c p) w"),
                          b * (2 * CHUNKS), first, (lambda: None) if last else next_x)
                if not first:
                    store(b - 1)
                    sp.wait_ge(out_stored, b * 16)
                else:
                    sp.dma_start(labels_sb[:, :], labels).then_inc(labels_loaded, 16)
                    sp.dma_start(g0_sb[:, :, :, :], g0_rows).then_inc(gate_weights_loaded, 16)
                    sp.dma_start(g1_sb[:, :, :], g1_rows).then_inc(gate_weights_loaded, 16)
                sp.dma_start(x_res[:, :, :], x_rows[bass.ds(b, 1)].rearrange("b p m d -> (b p) m d")
                             ).then_inc(x_res_loaded, 16)

            def expert_pass(b, slot, last=False):
                sp.wait_ge(labels_loaded, 16)
                label = sp.value_load(labels_sb[0:1, bass.ds(b, 1)], min_val=0, max_val=N_EXPERTS - 1)
                load_pass(lambda c: experts[bass.ds(label, 1), bass.ds(c, 1)].rearrange("e c p w -> (e c p) w"),
                          b * (2 * CHUNKS) + CHUNKS, False, lambda: None)

            def store(b):
                sp.wait_ge(mixed, b * 2 + 2)
                sp.dma_start(out[bass.ds(b, 1)].rearrange("b p m d -> (b p) m d"), mix[:, :, :]
                             ).then_inc(out_stored, 16)

            schedule(sp, shared_pass, expert_pass)
            for m in range(MC):
                sp.wait_ge(last_mixed, m + 1)
                sp.dma_start(out[BATCH - 1, :, m, :], mix[:, m, :]).then_inc(out_stored, 16)
            sp.wait_ge(out_stored, 16 * (BATCH - 1 + MC))

        @block.tensor
        def _(pe):
            def project_k(bank_, which, k, s, xslot):
                for n, (wp, xp) in enumerate(PASSES):
                    mm = nc.tensor.matmul(bank_[:, :], wi[s][wp][:, which, k, :], xs[xslot][xp][:, k, :],
                                          start=(n == 0 and k == 0), stop=(n == 2 and k == KC - 1))
                return mm

            def project_first():
                for k in range(KC):
                    pe.wait_ge(first_ready, k + 1)
                    pe.wait_ge(x_ready, k + 1)
                    gate_mm = project_k(ps_gate[0], 0, k, 0, 0)
                    lin_mm = project_k(ps_lin[0], 1, k, 0, 0)
                gate_mm.then_inc(gate_projected, 1)
                lin_mm.then_inc(lin_projected, 1)

            def project(t, s, xslot, second=False):
                pe.wait_ge(wi_ready, t)
                for which, bank_, free, done in ((0, ps_gate[s], gelu_done, gate_projected),
                                                 (1, ps_lin[s], product_done, lin_projected)):
                    if not second:
                        pe.wait_ge(free, t - 1)
                    for k in range(KC):
                        mm = project_k(bank_, which, k, s, xslot)
                    mm.then_inc(done, 1)

            def back_tile(m, s, start, stop):
                for n, (hp, wp) in enumerate(PASSES):
                    mm = nc.tensor.matmul(ps_out[m][:, :], hs[s][hp][:, m * P:(m + 1) * P], wo[s][wp][:, :],
                                          start=(start and n == 0), stop=(stop and n == 2), skip_group_check=True)
                return mm

            def wait_back(t):
                pe.wait_ge(hid_ready, t + 1)
                pe.wait_ge(wo_ready, t + 1)

            def back(t, s, start=False, stop=False):
                wait_back(t)
                for m in range(MC):
                    mm = back_tile(m, s, start, stop)
                mm.then_inc(down_done, 1)

            def last_chunks(t0, xslot):
                first_off = CHUNKS - PUT_OFF
                for c in range(first_off, CHUNKS):
                    project(t0 + c, c % 2, xslot)
                    if c == first_off:
                        back(t0 + c - 1, (c - 1) % 2)
                    else:
                        wait_back(t0 + c - 1)
                        back_tile(0, c - 1 - first_off, False, False)
                for s in range(BETWEEN):
                    back_tile(1, s, False, False)
                wait_back(t0 + CHUNKS - 1)
                back_tile(0, PUT_OFF - 1, False, True).then_inc(last_down_done, 1)
                for m in range(1, MC):
                    for s in range(BETWEEN if m == 1 else 0, PUT_OFF):
                        mm = back_tile(m, s, False, s == PUT_OFF - 1)
                    mm.then_inc(last_down_done, 1)

            def run_pass(number, xslot, next_xslot, next_batch, first=False, last=False):
                t0 = number * CHUNKS
                project(t0 + 1, 1, xslot, second=first)
                if not first:
                    pe.wait_ge(out_copied_act, number)
                    pe.wait_ge(out_copied_dve, number)
                back(t0, 0, start=True)
                with pe.Fori(1, (CHUNKS - PUT_OFF if last else CHUNKS) // 2) as j:
                    project(t0 + j * 2, 0, xslot)
                    back(t0 + j * 2 - 1, 1)
                    project(t0 + j * 2 + 1, 1, xslot)
                    back(t0 + j * 2, 0)
                if last:
                    last_chunks(t0, xslot)
                else:
                    if next_batch is not None:
                        pe.wait_ge(x_ready, (next_batch + 1) * KC)
                    project(t0 + CHUNKS, 0, next_xslot)
                    back(t0 + CHUNKS - 1, 1, stop=True)

            def shared_pass(b, slot, first=False, last=False):
                run_pass(b * 2, slot, slot, None, first)

            def expert_pass(b, slot, last=False):
                run_pass(b * 2 + 1, slot, 1 - slot, b + 1, last=last)

            pe.wait_ge(idle_ready, 1)
            for _ in range(IDLE_MATMULS):
                nc.tensor.matmul(ps_out[0][:, :], idle[:, 0:P], idle[:, :], start=True, stop=True)
            project_first()
            schedule(pe, shared_pass, expert_pass)

        @block.scalar
        def _(sc):
            def split_x(b, slot, k):
                sc.wait_ge(x_raw_loaded[k], b * 16 + 16)
                nc.scalar.copy(xs[slot][HI][:, k, :], x_raw[:, k, :]).then_inc(x_hi_done, 1)

            def split_wi(t, lap, r, free):
                sc.wait_ge(raw_loaded[r], lap * 16 + 16)
                if free:
                    sc.wait_ge(lin_projected, t - 1)
                nc.scalar.copy(wi[r % 2][HI][:, :, :, :].rearrange("p a k f -> p (a k f)"), raw[r][:, 0:WI]
                               ).then_inc(wi_hi_done, 1)

            def split_wo(t, r, slot, free):
                if free:
                    sc.wait_ge(down_done, t - 1)
                nc.scalar.copy(wo[slot][HI][:, :], raw[r][:, WI:CHUNK_W]).then_inc(wo_hi_done, 1)

            def chunk(t, lap, c, start=False, last=False):
                s, r, slot = c % 2, c % RAW_SLOTS, back_slot(c, last)
                sc.wait_ge(gate_projected, t + 1)
                if not start:
                    sc.wait_ge(product_done, t - 1)
                nc.scalar.activation(act[s][:, :], ps_gate[s][:, :], ACT.Gelu_apprx_tanh).then_inc(gelu_done, 1)
                sc.wait_ge(product_done, t + 1)
                if not start and slot < 2:
                    sc.wait_ge(down_done, t - 1)
                nc.scalar.copy(hs[slot][HI][:, :], hid[s][:, :]).then_inc(hid_hi_done, 1)
                if not last or c + 2 < CHUNKS:
                    split_wi(t + 2, lap + (r + 2) // RAW_SLOTS, (r + 2) % RAW_SLOTS, True)
                if not last or c + 1 < CHUNKS:
                    if start and c == 0:
                        sc.wait_ge(second_wo_loaded, 16)
                    next_slot = back_slot(c + 1, last)
                    split_wo(t + 1, (r + 1) % RAW_SLOTS, next_slot, not (start and c == 0) and next_slot < 2)

            def copy_out(number, dst):
                sc.wait_ge(down_done, number * CHUNKS + CHUNKS)
                for m in range(MC // 2):
                    last_ = nc.scalar.copy(dst[:, m, :], ps_out[m][:, :])
                last_.then_inc(out_copied_act, 1)

            def group(number, g, first=False, last=False, hooks={}):
                for r in range(RAW_SLOTS):
                    t = number * CHUNKS + g * RAW_SLOTS + r
                    chunk(t, number * GROUPS + g, g * RAW_SLOTS + r if last else r, first and r < 2, last)
                    if r in hooks:
                        hooks[r]()

            def exponentials(b):
                sc.wait_ge(logits_shifted, b + 1)
                nc.scalar.activation(gate_exp[:, :], logit_diff[:, :], ACT.Exp, accum_out=gate_den[:, :]
                                     ).then_inc(exp_done, 1)

            def shared_pass(b, slot, first=False, last=False):
                group(b * 2, 0, first, hooks={} if first else {0: lambda: copy_out(b * 2 - 1, e_out)})
                group(b * 2, 1, hooks={} if first else {2: lambda: exponentials(b - 1)})
                with sc.Fori(2, GROUPS) as g:
                    group(b * 2, g)

            def expert_pass(b, slot, last=False):
                group(b * 2 + 1, 0, hooks={0: lambda: copy_out(b * 2, s_out)})
                if not last:
                    for k in range(KC):
                        split_x(b + 1, 1 - slot, k)
                with sc.Fori(1, GROUPS - 2 if last else GROUPS) as g:
                    group(b * 2 + 1, g)
                if last:
                    for g in range(GROUPS - 2, GROUPS):
                        group(b * 2 + 1, g, last=True)

            first_wi = raw[0][:, 0:WI].rearrange("p (a k f) -> p a k f", a=2, k=KC)
            for k in range(KC):
                sc.wait_ge(first_loaded[k], 16)
                nc.scalar.copy(wi[0][HI][:, :, k, :], first_wi[:, :, k, :]).then_inc(first_hi_done, 1)
                split_x(0, 0, k)
            split_wi(1, 0, 1, False)
            sc.wait_ge(raw_loaded[0], 16)
            split_wo(0, 0, 0, False)
            schedule(sc, shared_pass, expert_pass)
            nc.scalar.activation(exp_warm[:, :], logits[:, 0:1], ACT.Exp)
            sc.wait_ge(last_down_done, 1)
            nc.scalar.copy(e_out[0:1, 0, :], ps_out[0][0:1, :]).then_inc(out_copied_act, 1)
            exponentials(BATCH - 1)
            sc.wait_ge(weight_step, BATCH * 2)
            for m in range(MC // 2, MC):
                nc.scalar.activation(s_out[:, m, :], s_out[:, m, :], ACT.Copy, scale=gate_w[:, SHARED:SHARED + 1]
                                     ).then_inc(last_scaled, 1)

        @block.vector
        def _(dve):
            def split_x(b, slot, k):
                dve.wait_ge(x_hi_done, b * KC + (k + 1))
                nc.vector.tensor_tensor(xs[slot][LO][:, k, :], x_raw[:, k, :], xs[slot][HI][:, k, :].bitcast(F32),
                                        ALU.subtract).then_inc(x_ready, 1)

            def split_wi(t, r):
                dve.wait_ge(wi_hi_done, t)
                flat = [wi[r % 2][p][:, :, :, :].rearrange("p a k f -> p (a k f)") for p in (HI, LO)]
                nc.vector.tensor_tensor(flat[LO], raw[r][:, 0:WI], flat[HI].bitcast(F32),
                                        ALU.subtract).then_inc(wi_ready, 1)

            def split_wo(t, r, slot):
                dve.wait_ge(wo_hi_done, t + 1)
                nc.vector.tensor_tensor(wo[slot][LO][:, :], raw[r][:, WI:CHUNK_W], wo[slot][HI][:, :].bitcast(F32),
                                        ALU.subtract).then_inc(wo_ready, 1)

            def chunk(t, c, last=False):
                s, r, slot = c % 2, c % RAW_SLOTS, back_slot(c, last)
                dve.wait_ge(lin_projected, t + 1)
                dve.wait_ge(gelu_done, t + 1)
                nc.vector.tensor_tensor(hid[s][:, :], act[s][:, :], ps_lin[s][:, :], ALU.mult
                                        ).then_inc(product_done, 1)
                dve.wait_ge(hid_hi_done, t + 1)
                nc.vector.tensor_tensor(hs[slot][LO][:, :], hid[s][:, :], hs[slot][HI][:, :].bitcast(F32), ALU.subtract
                                        ).then_inc(hid_ready, 1)
                if not last or c + 2 < CHUNKS:
                    split_wi(t + 2, (r + 2) % RAW_SLOTS)
                if not last or c + 1 < CHUNKS:
                    split_wo(t + 1, (r + 1) % RAW_SLOTS, back_slot(c + 1, last))

            def copy_out(number, dst):
                dve.wait_ge(down_done, number * CHUNKS + CHUNKS)
                for m in range(MC // 2, MC):
                    last_ = nc.vector.tensor_copy(dst[:, m, :], ps_out[m][:, :])
                last_.then_inc(out_copied_dve, 1)

            def group(number, g, last=False, hooks={}):
                for r in range(RAW_SLOTS):
                    chunk(number * CHUNKS + g * RAW_SLOTS + r, g * RAW_SLOTS + r if last else r, last)
                    if r in hooks:
                        hooks[r]()

            def gate_shared(b):
                dve.wait_ge(gate_weights_loaded, 32)
                dve.wait_ge(row_spread, b * 2 + 1)
                for c in range(NC):
                    last_ = nc.vector.tensor_tensor_reduce(gate_prod[:, c, :], g0_sb[:, c, SHARED, :], gate_row[:, 0, :],
                                                           1.0, 0.0, ALU.mult, ALU.add, gate_sum[:, 0, c:c + 1])
                last_.then_inc(gate_step, 1)

            def gate_expert(b):
                dve.wait_ge(row_spread, b * 2 + 2)
                dve.wait_ge(gate_step, b * 3 + 1)
                for c in range(NC):
                    last_ = nc.vector.tensor_tensor_reduce(gate_prod[:, c, :], g0_sb[:, c, EXPERT, :], gate_row[:, 1, :],
                                                           1.0, gate_sum[:, 0, c:c + 1], ALU.mult, ALU.add,
                                                           gate_sum[:, 1, c:c + 1])
                last_.then_inc(gate_step, 1)
                dve.wait_ge(gate_step, b * 3 + 2)
                nc.vector.tensor_scalar(gate_act[:, :], gate_sum[:, 1, :], 0.0, None, ALU.max).then_inc(gate_step, 1)
                dve.wait_ge(gate_step, b * 3 + 3)
                for c in range(2):
                    nc.vector.tensor_tensor_reduce(logit_prod[:, c, :], g1_sb[:, c, :], gate_act[:, :], 1.0, 0.0,
                                                   ALU.mult, ALU.add, logit_part[:, c:c + 1]
                                                   ).then_inc(logits_part_done, 1)

            def shift_logits(b):
                dve.wait_ge(logits_done, b + 1)
                nc.vector.tensor_reduce(logit_max[:, :], logits[:, :], AX.X, ALU.max).then_inc(max_done, 1)
                dve.wait_ge(max_done, b + 1)
                nc.vector.tensor_scalar(logit_diff[:, :], logits[:, :], logit_max[:, 0:1], None, ALU.subtract
                                        ).then_inc(logits_shifted, 1)

            def gate_weights(b):
                dve.wait_ge(exp_done, b + 1)
                nc.vector.reciprocal(gate_inv[:, :], gate_den[:, :]).then_inc(weight_step, 1)
                dve.wait_ge(weight_step, b * 2 + 1)
                nc.vector.tensor_scalar(gate_w[:, :], gate_exp[:, :], gate_inv[:, 0:1], None, ALU.mult
                                        ).then_inc(weight_step, 1)

            def combine(b):
                dve.wait_ge(weight_step, b * 2 + 2)
                dve.wait_ge(x_res_loaded, b * 16 + 16)
                dve.wait_ge(out_copied_act, b * 2 + 2)
                nc.vector.scalar_tensor_tensor(mix[:, :, :], s_out[:, :, :], gate_w[:, SHARED:SHARED + 1], x_res[:, :, :],
                                               ALU.mult, ALU.add).then_inc(mixed, 1)
                dve.wait_ge(mixed, b * 2 + 1)
                nc.vector.scalar_tensor_tensor(mix[:, :, :], e_out[:, :, :], gate_w[:, EXPERT:EXPERT + 1], mix[:, :, :],
                                               ALU.mult, ALU.add).then_inc(mixed, 1)

            def shared_pass(b, slot, first=False, last=False):
                group(b * 2, 0, hooks={} if first else {0: lambda: copy_out(b * 2 - 1, e_out),
                                                        3: lambda: gate_expert(b - 1)})
                group(b * 2, 1, hooks={} if first else {1: lambda: shift_logits(b - 1)})
                if not first:
                    gate_weights(b - 1)
                    combine(b - 1)
                with dve.Fori(2, GROUPS) as g:
                    group(b * 2, g)

            def expert_pass(b, slot, last=False):
                group(b * 2 + 1, 0, hooks={0: lambda: copy_out(b * 2, s_out)})
                if not last:
                    for k in range(KC):
                        split_x(b + 1, 1 - slot, k)
                group(b * 2 + 1, 1)
                gate_shared(b)
                if last:
                    for g in range(GROUPS - 2, GROUPS):
                        group(b * 2 + 1, g, last=True)
                else:
                    with dve.Fori(2, GROUPS) as g:
                        group(b * 2 + 1, g)

            nc.vector.memset(idle[:, :], 0.0).then_inc(idle_ready, 1)
            first_wi = raw[0][:, 0:WI].rearrange("p (a k f) -> p a k f", a=2, k=KC)
            for k in range(KC):
                dve.wait_ge(first_hi_done, k + 1)
                nc.vector.tensor_tensor(wi[0][LO][:, :, k, :], first_wi[:, :, k, :],
                                        wi[0][HI][:, :, k, :].bitcast(F32), ALU.subtract).then_inc(first_ready, 1)
                split_x(0, 0, k)
            split_wi(1, 1)
            split_wo(0, 0, 0)
            schedule(dve, shared_pass, expert_pass)
            gate_expert(BATCH - 1)
            shift_logits(BATCH - 1)
            gate_weights(BATCH - 1)
            dve.wait_ge(weight_step, BATCH * 2)
            dve.wait_ge(x_res_loaded, BATCH * 16)
            for m in range(MC // 2):
                nc.vector.scalar_tensor_tensor(s_out[:, m, :], s_out[:, m, :], gate_w[:, SHARED:SHARED + 1],
                                               x_res[:, m, :], ALU.mult, ALU.add).then_inc(last_based_dve, 1)
            for m in range(MC):
                if m < MC // 2:
                    dve.wait_ge(last_based_dve, m + 1)
                else:
                    dve.wait_ge(last_based_pool, m + 1 - MC // 2)
                dve.wait_ge(last_down_done, m + 1)
                nc.vector.scalar_tensor_tensor(mix[:, m, :], ps_out[m][:, :], gate_w[:, EXPERT:EXPERT + 1],
                                               s_out[:, m, :], ALU.mult, ALU.add).then_inc(last_mixed, 1)

        @block.gpsimd
        def _(pool):
            for b in range(BATCH):
                for n, net_out in enumerate((s_out, e_out)):
                    pool.wait_ge(out_copied_act, b * 2 + (n + 1))
                    nc.gpsimd.partition_broadcast(gate_row[:, n, :], net_out[0:1, 0, :]).then_inc(row_spread, 1)
                pool.wait_ge(logits_part_done, b * 2 + 2)
                nc.gpsimd.partition_all_reduce(logits[:, :], logit_part[:, :], P, RADD).then_inc(logits_done, 1)
            pool.wait_ge(x_res_loaded, BATCH * 16)
            for m in range(MC // 2, MC):
                pool.wait_ge(last_scaled, m + 1 - MC // 2)
                nc.gpsimd.tensor_tensor(s_out[:, m, :], x_res[:, m, :], s_out[:, m, :], ALU.add
                                        ).then_inc(last_based_pool, 1)


def kernel(x, itok_B_0_2, L0_cond_Wi0, L0_cond_Wi1, L0_cond_Wo, L0_cond_sWi0, L0_cond_sWi1, L0_cond_sWo,
           L0_cond_g0, L0_cond_g1):
    import numpy as np
    import concourse.bacc as bacc
    from concourse import mybir as mb
    from concourse.bass_utils import run_bass_kernel_spmd

    x, labels = np.asarray(x), np.asarray(itok_B_0_2)
    BATCH, TOK, D = x.shape
    E, _, F = L0_cond_Wi0.shape
    KC, MC, CHUNKS, NC = D // P, TOK // P, F // P, D // P

    def chunked(wi0, wi1, wo):
        n = wi0.shape[0]
        ups = [np.asarray(w).reshape(n, KC, P, CHUNKS, P).transpose(0, 3, 2, 1, 4).reshape(n, CHUNKS, P, D)
               for w in (wi0, wi1)]
        return np.ascontiguousarray(np.concatenate(ups + [np.asarray(wo).reshape(n, CHUNKS, P, D)], axis=-1))

    by_row = x.reshape(BATCH, P, MC, D)
    arrays = {
        "x_cols": by_row.reshape(BATCH, P, MC, KC, P).transpose(0, 4, 3, 2, 1).reshape(BATCH, P, KC, TOK),
        "x_rows": by_row,
        "labels": labels.reshape(1, BATCH),
        "experts": chunked(L0_cond_Wi0, L0_cond_Wi1, L0_cond_Wo),
        "shared": chunked(*(np.asarray(w)[None] for w in (L0_cond_sWi0, L0_cond_sWi1, L0_cond_sWo)))[0],
        "g0_rows": np.asarray(L0_cond_g0).reshape(2, D, NC, P).transpose(3, 2, 0, 1),
        "g1_rows": np.asarray(L0_cond_g1).reshape(NC, P, 2).transpose(1, 2, 0),
    }
    arrays = {name: np.ascontiguousarray(a) for name, a in arrays.items()}

    nc = bacc.Bacc("TRN2", target_bir_lowering=False, num_devices=1)
    args = [nc.dram_tensor(name, a.shape, mb.dt.from_np(a.dtype), kind="ExternalInput").ap()
            for name, a in arrays.items()]
    out = nc.dram_tensor("out", by_row.shape, mb.dt.from_np(x.dtype), kind="ExternalOutput").ap()
    build(nc, *args, out)
    results = run_bass_kernel_spmd(nc, [arrays], core_ids=[0])
    return results.results[0]["out"].reshape(x.shape)
```
